# Optimizing a Trainium2 kernel written in Bass

```python
import numpy as np
import jax
import jax.numpy as jnp

def _softmax(x, axis=-1):
    return jax.nn.softmax(x, axis=axis)

def _gelu(x):
    return jax.nn.gelu(x, approximate=True)

def _silu(x):
    return jax.nn.silu(x)

def _sigmoid(x):
    return jax.nn.sigmoid(x)

def _layernorm(x, axis=-1, eps=1e-05):
    m = jnp.mean(x, axis=axis, keepdims=True)
    v = jnp.var(x, axis=axis, keepdims=True)
    return (x - m) / jnp.sqrt(v + eps)

def _scatter_add(tgt, idx, src, axis=0):
    return tgt.at[idx].add(src)

def _segment_sum(src, seg, n):
    return jax.ops.segment_sum(src, seg, n)
kernel_name = 'mk_cond_resid_d1_seqx_r4_f2d16c'

def setup_inputs(seed: int=0):
    np.random.seed(seed)
    _w = jnp.asarray

    def _rec_inputs():
        import jax
        import jax.numpy as jnp
        _rk = jax.random.key(seed)
        x = -0.000125 + 0.9999 * jax.random.normal(jax.random.fold_in(_rk, 1), (8, 512, 256), jnp.float32)
        _lenS = 512 - jax.random.randint(jax.random.fold_in(_rk, 7), (8,), 0, max(1, 512 // 4) + 1, jnp.int32)
        _lenS2 = 512 - jax.random.randint(jax.random.fold_in(_rk, 8), (8,), 0, max(1, 512 // 4) + 1, jnp.int32)
        cond_1024 = -0.00493535 + 1.00056 * jax.random.normal(jax.random.fold_in(_rk, 11), (8, 256), jnp.float32)
        return (x, cond_1024)
    x, cond_1024 = _rec_inputs()

    def _L0_cond_setup():
        import jax, jax.numpy as jnp
        import numpy as np
        INPUT_DIM = 256
        LATENT_DIM = 256
        key = jax.random.key(seed)
        ks = jax.random.split(key, 8)
        B, T = (64, 128)
        concat_dim = INPUT_DIM + LATENT_DIM
        s = lambda fan_in: 1.0 / np.sqrt(fan_in)
        return {'x': jax.random.normal(ks[0], (B, T, INPUT_DIM), dtype=jnp.float32), 'h0': jax.random.normal(ks[1], (B, LATENT_DIM), dtype=jnp.float32), 'w_W': jax.random.uniform(ks[2], (concat_dim, 2 * LATENT_DIM), jnp.float32, -s(concat_dim), s(concat_dim)), 'w_b': jax.random.uniform(ks[3], (2 * LATENT_DIM,), jnp.float32, -s(concat_dim), s(concat_dim)), 'wx_W': jax.random.uniform(ks[4], (INPUT_DIM, LATENT_DIM), jnp.float32, -s(INPUT_DIM), s(INPUT_DIM)), 'wx_b': jax.random.uniform(ks[5], (LATENT_DIM,), jnp.float32, -s(INPUT_DIM), s(INPUT_DIM)), 'wh_W': jax.random.uniform(ks[6], (LATENT_DIM, LATENT_DIM), jnp.float32, -s(LATENT_DIM), s(LATENT_DIM)), 'wh_b': jax.random.uniform(ks[7], (LATENT_DIM,), jnp.float32, -s(LATENT_DIM), s(LATENT_DIM))}
    _L0_cond_all = _L0_cond_setup()
    _L0_cond_in = {k: v for k, v in _L0_cond_all.items() if k in ('w_W', 'w_b', 'wx_W', 'wx_b', 'wh_W', 'wh_b')}
    del _L0_cond_all
    return {'x': x, 'cond_1024': cond_1024, 'L0_cond_w_W': _L0_cond_in['w_W'], 'L0_cond_w_b': _L0_cond_in['w_b'], 'L0_cond_wx_W': _L0_cond_in['wx_W'], 'L0_cond_wx_b': _L0_cond_in['wx_b'], 'L0_cond_wh_W': _L0_cond_in['wh_W'], 'L0_cond_wh_b': _L0_cond_in['wh_b']}

def reference(x, cond_1024, L0_cond_w_W, L0_cond_w_b, L0_cond_wx_W, L0_cond_wx_b, L0_cond_wh_W, L0_cond_wh_b):
    import jax
    import jax.numpy as jnp

    def _L0_cond_ref(x, h0, w_W, w_b, wx_W, wx_b, wh_W, wh_b):
        import jax, jax.numpy as jnp
        import numpy as np
        INPUT_DIM = 256
        LATENT_DIM = 256
        xT = jnp.swapaxes(x, 0, 1)

        def step(h, x_t):
            fused = jax.nn.sigmoid(jnp.concatenate([x_t, h], axis=-1) @ w_W + w_b)
            hidden_state, output_state = jnp.split(fused, 2, axis=-1)
            memory_state = x_t @ wx_W + wx_b + hidden_state * (h @ wh_W + wh_b)
            h_new = output_state * h + (1.0 - output_state) * jnp.tanh(memory_state)
            return (h_new, h_new)
        _, hs = jax.lax.scan(step, h0, xT)
        return jnp.swapaxes(hs, 0, 1)
    x = x + _L0_cond_ref(x, cond_1024, L0_cond_w_W, L0_cond_w_b, L0_cond_wx_W, L0_cond_wx_b, L0_cond_wh_W, L0_cond_wh_b)
    return x

_drawn_inputs = setup_inputs


def setup_inputs(seed=0):
    import zlib

    import numpy as np

    out = dict(_drawn_inputs(seed))
    spreads = {}
    factors = {'L0_cond_w_b': 8.0, 'L0_cond_wh_b': 3.805}
    for name, (base, spread) in spreads.items():
        noise = np.random.default_rng([zlib.crc32(name.encode()), seed]).standard_normal(out[name].shape)
        drawn = base * np.exp(spread * noise) if base else spread * noise
        out[name] = jnp.asarray(drawn.astype(out[name].dtype))
    for name, factor in factors.items():
        out[name] = (out[name] * factor).astype(out[name].dtype)
    return out
```

```python
import concourse.bass as bass
from concourse import mybir
from contextlib import ExitStack


def gated_recurrence(nc, x, h0, w_state, w_input, bias, out):
    fp32 = mybir.dt.float32
    bf16 = mybir.dt.bfloat16
    ALU = mybir.AluOpType
    ACT = mybir.ActivationFunctionType
    AX = mybir.AxisListType

    P = 128
    B = h0.shape[2]
    KC = h0.shape[1]
    G = KC * B
    T = x.shape[1] // G
    PARTS = 3
    GATES = w_state.shape[2] // (KC * P)
    R, Z, C = range(GATES)
    SLOTS = 4
    GROUP = 4
    BLOCK = 2 * GROUP
    NB = T // BLOCK
    HW = 3 * G + 4

    ctx = ExitStack()
    with ctx:
        def sb(name, shape, dt):
            return ctx.enter_context(nc.sbuf_tensor(name, shape, dt))

        def sem(name):
            return ctx.enter_context(nc.semaphore(name))

        X = sb("X", [P, NB + 1, BLOCK * G], fp32)
        xsplit = sb("xsplit", [P, 2, PARTS, GROUP * G], fp32)
        ws32 = sb("ws32", [P, KC, GATES * KC * P], fp32)
        wi32 = sb("wi32", [P, KC, GATES * KC * P], fp32)
        ws = sb("ws", [P, PARTS, KC, GATES * KC * P], bf16)
        wi = sb("wi", [P, PARTS, KC, GATES * KC * P], bf16)
        bias32 = sb("bias32", [P, (GATES + 1) * KC * P], fp32)
        bparts = sb("bparts", [P, PARTS, (GATES + 1) * KC * P], bf16)
        brows = sb("brows", [P, (GATES + 1) * KC * P], bf16)
        ones = sb("ones", [P, GROUP * B], bf16)
        hist = sb("hist", [P, 2, PARTS, HW], fp32)
        h0_sb = sb("h0_sb", [P, G], fp32)
        reset_row = sb("reset_row", [P, SLOTS * G], fp32)
        update_row = sb("update_row", [P, 3 * G], fp32)

        bank_r = [ctx.enter_context(nc.psum_tensor(f"bank_r{i}", [P, 512], fp32)) for i in range(2)]
        bank_z = [ctx.enter_context(nc.psum_tensor(f"bank_z{i}", [P, 512], fp32)) for i in range(2)]
        bank_c = [ctx.enter_context(nc.psum_tensor(f"bank_c{i}", [P, 512], fp32)) for i in range(2)]
        bank_m = ctx.enter_context(nc.psum_tensor("bank_m", [P, 512], fp32))
        bank_zs = ctx.enter_context(nc.psum_tensor("bank_zs", [P, 512], fp32))

        weights_in = [sem(f"weights_in{i}") for i in range(2)]
        small_in = sem("small_in")
        x_in = sem("x_in")
        bias_zeroed = sem("bias_zeroed")
        consts_ready = sem("consts_ready")
        split_act = sem("split_act")
        split_dve = sem("split_dve")
        weights_split = sem("weights_split")
        input_copied = sem("input_copied")
        input_mid = sem("input_mid")
        input_split = sem("input_split")
        state_ready = sem("state_ready")
        mid_ready = sem("mid_ready")
        low_ready = sem("low_ready")
        reset_summed = sem("reset_summed")
        hidden_summed = sem("hidden_summed")
        update_summed = sem("update_summed")
        reset_ready = sem("reset_ready")
        memory_ready = sem("memory_ready")
        update_reduced = sem("update_reduced")
        update_ready = sem("update_ready")
        candidate_ready = sem("candidate_ready")
        y_ready = sem("y_ready")
        y_out = sem("y_out")

        block = ctx.enter_context(nc.Block())

        def state(q, part=0):
            return hist[:, q, part, 2:2 + 3 * G:3]

        def upper(words):
            return words.bitcast(bf16)[:, 1::2]

        def state_upper(q, part):
            return hist[:, q, part, :].bitcast(bf16)[:, 5:5 + 6 * G:6]

        @block.sync
        def _(sp):
            sp.dma_start(ws32[:, :, :], w_state).then_inc(weights_in[0], 16)
            sp.dma_start(wi32[:, :, :], w_input).then_inc(weights_in[1], 16)
            for n in range(2):
                sp.dma_start(X[:, n * NB // 2:(n + 1) * NB // 2, :],
                             x[:, n * T * G // 2:(n + 1) * T * G // 2].rearrange("p (n c) -> p n c", c=BLOCK * G)
                             ).then_inc(x_in, 16)
            with sp.Fori(0, NB) as n:
                sp.wait_ge(y_ready, n * BLOCK + BLOCK)
                sp.dma_start(out[:, bass.ds(n * (BLOCK * G), BLOCK * G)],
                             X[:, bass.ds(n, 1), :].rearrange("p a c -> p (a c)")).then_inc(y_out, 16)
            sp.wait_ge(y_out, 16 * NB)

        @block.gpsimd
        def _(pool):
            nc.gpsimd.memset(bias32[:, :], 0.0).then_inc(bias_zeroed, 1)
            nc.gpsimd.memset(brows[:, :], 0.0).then_inc(consts_ready, 1)
            nc.gpsimd.memset(ones[:, :], 1.0).then_inc(consts_ready, 1)
            nc.gpsimd.memset(reset_row[:, :], 1.0).then_inc(bias_zeroed, 1)
            nc.gpsimd.memset(update_row[:, :], 0.0).then_inc(bias_zeroed, 1)
            pool.wait_ge(bias_zeroed, 3)
            nc.gpsimd.memset(reset_row[:, 0::SLOTS], 0.0).then_inc(consts_ready, 1)
            nc.gpsimd.memset(update_row[:, 1::3], -1.0).then_inc(consts_ready, 1)
            nc.gpsimd.memset(X[:, NB, :], 0.0).then_inc(consts_ready, 1)
        CONSTS = 5

        @block.scalar
        def _(act):
            act.dma_start(h0_sb[:, :], h0.rearrange("p k b -> p (k b)")).then_inc(small_in, 16)
            act.wait_ge(bias_zeroed, 1)
            for i in range(PARTS):
                act.dma_start(bias32[32 * i:32 * i + 1, :], bias).then_inc(small_in, 16)

            def first_part(parts, words, done):
                nc.scalar.activation(parts, words, ACT.Copy).then_inc(split_act, 1)

            act.wait_ge(small_in, 16 * (1 + PARTS))
            first_part(bparts[:, 0, :], bias32[:, :], 1)
            act.wait_ge(weights_in[0], 16)
            first_part(ws[:, 0], ws32[:, :, :], 2)
            act.wait_ge(weights_in[1], 16)
            first_part(wi[:, 0], wi32[:, :, :], 3)
            for i, (parts, words) in enumerate([(bparts[:, 1, :], bias32[:, :]), (ws[:, 1], ws32[:, :, :]),
                                                (wi[:, 1], wi32[:, :, :])]):
                act.wait_ge(split_dve, i + 1)
                nc.scalar.activation(parts, words, ACT.Copy).then_inc(split_act, 1)
            act.wait_ge(x_in, 32)
            for g in range(2):
                nc.scalar.activation(xsplit[:, g, 0, :], X[:, 0, g * GROUP * G:(g + 1) * GROUP * G],
                                     ACT.Copy).then_inc(input_copied, 1)
            act.wait_ge(consts_ready, CONSTS)

            with act.Fori(0, NB) as n:
                for s in range(BLOCK):
                    q, par = s % 2, s // GROUP
                    g = s // GROUP
                    if s % GROUP == 1:
                        nc.scalar.activation(
                            xsplit[:, g, 0, :],
                            X[:, bass.ds(n + 1, 1), g * GROUP * G:(g + 1) * GROUP * G].rearrange("p a c -> p (a c)"),
                            ACT.Copy).then_inc(input_copied, 1)
                    act.wait_ge(reset_summed, n * BLOCK + (s + 1))
                    nc.scalar.activation(reset_row[:, SLOTS - 1::SLOTS],
                                         bank_r[par][:, (s % GROUP) * G:(s % GROUP + 1) * G],
                                         ACT.Sigmoid).then_inc(reset_ready, 1)
                    act.wait_ge(memory_ready, n * BLOCK + (s + 1))
                    nc.scalar.activation(
                        hist[:, q, 0, 1:1 + 3 * G].rearrange("p (g k) -> p g k", k=3)[:, :, 0::2],
                        bank_m[:, SLOTS - 1:SLOTS * G:SLOTS].unsqueeze(2).to_broadcast([P, G, 2]),
                        ACT.Tanh).then_inc(candidate_ready, 1)
                    act.wait_ge(update_reduced, n * BLOCK + (s + 1))
                    nc.scalar.activation(update_row[:, 2::3], bank_zs[:, 0:G], ACT.Sigmoid).then_inc(update_ready, 1)

        @block.vector
        def _(dve):
            both = [(bparts[:, 0, :], bparts[:, 1, :], bparts[:, 2, :], bias32[:, :]),
                    (ws[:, 0], ws[:, 1], ws[:, 2], ws32[:, :, :]),
                    (wi[:, 0], wi[:, 1], wi[:, 2], wi32[:, :, :])]
            for i, (hi, mid, lo, words) in enumerate(both):
                dve.wait_ge(split_act, i + 1)
                nc.vector.tensor_tensor(words, words, hi, ALU.subtract).then_inc(split_dve, 1)
            for i, (hi, mid, lo, words) in enumerate(both):
                dve.wait_ge(split_act, len(both) + i + 1)
                nc.vector.tensor_tensor(lo, words, mid, ALU.subtract).then_inc(split_dve, 1)
            dve.wait_ge(split_dve, 2 * len(both))
            dve.wait_ge(consts_ready, CONSTS)
            for i in range(PARTS):
                nc.vector.tensor_copy(brows[32 * i:32 * i + 1, :], bparts[32 * i:32 * i + 1, i, :]
                                      ).then_inc(weights_split, 1)
            for g in range(2):
                dve.wait_ge(input_copied, g + 1)
                nc.vector.tensor_tensor(xsplit[:, g, 1, :], xsplit[:, g, 0, :], upper(xsplit[:, g, 0, :]),
                                        ALU.subtract).then_inc(input_mid, 1)
                dve.wait_ge(input_mid, g + 1)
                nc.vector.tensor_tensor(xsplit[:, g, 2, :], xsplit[:, g, 1, :], upper(xsplit[:, g, 1, :]),
                                        ALU.subtract).then_inc(input_split, 1)
            dve.wait_ge(small_in, 16 * (1 + PARTS))
            nc.vector.tensor_copy(state(0), h0_sb[:, :]).then_inc(state_ready, 1)
            dve.wait_ge(state_ready, 1)
            nc.vector.tensor_tensor(state(0, 1), state(0), state_upper(0, 0), ALU.subtract).then_inc(mid_ready, 1)
            dve.wait_ge(mid_ready, 1)
            nc.vector.tensor_tensor(state(0, 2), state(0, 1), state_upper(0, 1), ALU.subtract).then_inc(low_ready, 1)

            with dve.Fori(0, NB) as n:
                for s in range(BLOCK):
                    q, par, new = s % 2, s // GROUP, 1 - s % 2
                    g = s // GROUP
                    dve.wait_ge(hidden_summed, n * BLOCK + (s + 1))
                    dve.wait_ge(reset_ready, n * BLOCK + (s + 1))
                    cols = (s % GROUP) * G * SLOTS
                    nc.vector.tensor_tensor_scan(bank_m[:, 0:SLOTS * G], reset_row[:, :],
                                                 bank_c[par][:, cols:cols + SLOTS * G], 0.0,
                                                 ALU.mult, ALU.add).then_inc(memory_ready, 1)
                    dve.wait_ge(update_summed, n * BLOCK + (s + 1))
                    cols = (s % GROUP) * G * PARTS
                    nc.vector.tensor_reduce(
                        bank_zs[:, 0:G],
                        bank_z[par][:, cols:cols + PARTS * G].rearrange("p (k c) -> p c k", k=PARTS),
                        AX.X, ALU.add).then_inc(update_reduced, 1)
                    dve.wait_ge(candidate_ready, n * BLOCK + (s + 1))
                    dve.wait_ge(update_ready, n * BLOCK + (s + 1))
                    nc.vector.tensor_tensor_scan(hist[:, new, 0, 0:3 * G], update_row[:, :],
                                                 hist[:, q, 0, 1:1 + 3 * G], 0.0,
                                                 ALU.mult, ALU.add).then_inc(state_ready, 1)
                    dve.wait_ge(state_ready, n * BLOCK + (s + 2))
                    nc.vector.tensor_tensor(state(new, 1), state(new), state_upper(new, 0),
                                            ALU.subtract).then_inc(mid_ready, 1)
                    dve.wait_ge(mid_ready, n * BLOCK + (s + 2))
                    nc.vector.tensor_tensor(state(new, 2), state(new, 1), state_upper(new, 1),
                                            ALU.subtract).then_inc(low_ready, 1)
                    y = X[:, bass.ds(n, 1), s * G:(s + 1) * G].rearrange("p a c -> p (a c)")
                    nc.vector.tensor_tensor(y, y, state(new), ALU.add).then_inc(y_ready, 1)
                    if s % GROUP == 1:
                        dve.wait_ge(input_copied, n * 2 + (g + 3))
                        nc.vector.tensor_tensor(xsplit[:, g, 1, :], xsplit[:, g, 0, :], upper(xsplit[:, g, 0, :]),
                                                ALU.subtract).then_inc(input_mid, 1)
                    if s % GROUP == 2:
                        dve.wait_ge(input_mid, n * 2 + (g + 3))
                        nc.vector.tensor_tensor(xsplit[:, g, 2, :], xsplit[:, g, 1, :], upper(xsplit[:, g, 1, :]),
                                                ALU.subtract).then_inc(input_split, 1)

        @block.tensor
        def _(pe):
            def weights(w, part, kc, gate, o):
                c = (gate * KC + o) * P
                return w[:, part, kc, c:c + P]

            def state_part(q, part, kc):
                return hist[:, q, part, :].bitcast(bf16)[:, 5 + 6 * B * kc:5 + 6 * B * kc + 6 * B:6]

            def state_parts(q, kc):
                return hist[:, q, :, :].bitcast(bf16)[:, :, 5 + 6 * B * kc:5 + 6 * B * kc + 6 * B:6]

            def input_part(g, part, kc):
                return xsplit[:, g, part, :].rearrange("p (t k b) -> p t k b", k=KC, b=B)[:, :, kc, :].bitcast(bf16)[:, :, 1::2]

            def in_group(gate, par, o, slot=0):
                if gate == R:
                    return bank_r[par][:, 0:GROUP * G].rearrange("p (t o b) -> p t o b", o=KC, b=B)[:, :, o, :]
                if gate == Z:
                    v = bank_z[par][:, 0:GROUP * PARTS * G].rearrange("p (t k o b) -> p t k o b", k=PARTS, o=KC, b=B)
                    return v[:, :, 0, o, :]
                v = bank_c[par][:, 0:GROUP * SLOTS * G].rearrange("p (t o b k) -> p t o b k", o=KC, b=B, k=SLOTS)
                return v[:, :, o, :, slot]

            PAIRS = [(2, 0), (1, 1), (0, 2), (1, 0), (0, 1), (0, 0)]

            def input_products(g, par):
                for gate, row, slot in ((R, 0, 0), (Z, 1, 0), (C, 2, 0), (C, 3, SLOTS - 1)):
                    for o in range(KC):
                        yield (in_group(gate, par, o, slot), brows[:, (row * KC + o) * P:(row * KC + o + 1) * P],
                               ones[:, :], o == 0 and slot == 0)
                for gate in (R, Z, C):
                    for o in range(KC):
                        for kc in range(KC):
                            for i, j in PAIRS:
                                yield (in_group(gate, par, o, SLOTS - 1), weights(wi, i, kc, gate, o),
                                       input_part(g, j, kc), False)

            def issue(product):
                to, stationary, moving, first = product
                nc.tensor.matmul(to, stationary, moving, start=first, stop=True, skip_group_check=True)

            pe.wait_ge(weights_split, PARTS)
            pe.wait_ge(input_split, 1)
            for product in input_products(0, 0):
                issue(product)

            with pe.Fori(0, NB) as n:
                for s in range(BLOCK):
                    q, par, s4 = s % 2, s // GROUP, s % GROUP
                    if s4 == 0:
                        ahead = list(input_products(1 - par, 1 - par))
                        each = len(ahead) // GROUP

                    def reset_sums(i, j):
                        for o in range(KC):
                            for kc in range(KC):
                                c = s4 * G + o * B
                                last = nc.tensor.matmul(bank_r[par][:, c:c + B], weights(ws, i, kc, R, o),
                                                        state_part(q, j, kc), start=False, stop=True,
                                                        skip_group_check=True)
                        return last

                    pe.wait_ge(state_ready, n * BLOCK + (s + 1))
                    for i in (2, 1, 0):
                        reset_sums(i, 0)
                    pe.wait_ge(mid_ready, n * BLOCK + (s + 1))
                    for i in (1, 0):
                        reset_sums(i, 1)
                    pe.wait_ge(low_ready, n * BLOCK + (s + 1))
                    reset_sums(0, 2).then_inc(reset_summed, 1)
                    hidden = bank_c[par][:, s4 * SLOTS * G:(s4 + 1) * SLOTS * G].rearrange(
                        "p (o b k) -> p o k b", o=KC, k=SLOTS)
                    for o in range(KC):
                        for kc in range(KC):
                            for i in (2, 1, 0):
                                last = nc.tensor.matmul(hidden[:, o, 0:PARTS, :], weights(ws, i, kc, C, o),
                                                        state_parts(q, kc), start=False, stop=True,
                                                        skip_group_check=True)
                    last.then_inc(hidden_summed, 1)
                    update = bank_z[par][:, s4 * PARTS * G:(s4 + 1) * PARTS * G].rearrange(
                        "p (k o b) -> p o k b", o=KC, k=PARTS)
                    for o in range(KC):
                        for kc in range(KC):
                            for i in (2, 1, 0):
                                last = nc.tensor.matmul(update[:, o, :, :], weights(ws, i, kc, Z, o),
                                                        state_parts(q, kc), start=False, stop=True,
                                                        skip_group_check=True)
                    last.then_inc(update_summed, 1)
                    if s4 == 0:
                        pe.wait_ge(input_split, n * 2 + (par + 2))
                    for product in ahead[s4 * each:(s4 + 1) * each]:
                        issue(product)


def kernel(x, cond_1024, L0_cond_w_W, L0_cond_w_b, L0_cond_wx_W, L0_cond_wx_b, L0_cond_wh_W, L0_cond_wh_b):
    import numpy as np
    import concourse.bacc as bacc
    from concourse.bass_utils import run_bass_kernel_spmd

    x, h0 = np.asarray(x), np.asarray(cond_1024)
    w_W, w_b = np.asarray(L0_cond_w_W), np.asarray(L0_cond_w_b)
    wx_W, wx_b = np.asarray(L0_cond_wx_W), np.asarray(L0_cond_wx_b)
    wh_W, wh_b = np.asarray(L0_cond_wh_W), np.asarray(L0_cond_wh_b)
    B, T, D = x.shape
    P = 128
    KC = D // P

    def rows(w):
        return np.ascontiguousarray(w.reshape(KC, P, -1).transpose(1, 0, 2))

    arrays = {
        "x": np.ascontiguousarray(x.reshape(B, T, KC, P).transpose(3, 1, 2, 0).reshape(P, T * KC * B)),
        "h0": np.ascontiguousarray(h0.reshape(B, KC, P).transpose(2, 1, 0)),
        "w_state": rows(np.concatenate([w_W[D:], wh_W], axis=1)),
        "w_input": rows(np.concatenate([w_W[:D], wx_W], axis=1)),
        "bias": np.ascontiguousarray(np.concatenate([w_b, wh_b, wx_b])[None, :]),
    }
    nc = bacc.Bacc("TRN2", target_bir_lowering=False, num_devices=1)
    args = [nc.dram_tensor(name, a.shape, mybir.dt.from_np(a.dtype), kind="ExternalInput").ap()
            for name, a in arrays.items()]
    out = nc.dram_tensor("y", arrays["x"].shape, mybir.dt.float32, kind="ExternalOutput").ap()
    gated_recurrence(nc, *args, out)
    r = run_bass_kernel_spmd(nc, [arrays], core_ids=[0])
    y = r.results[0]["y"]
    return np.ascontiguousarray(y.reshape(P, T, KC, B).transpose(3, 1, 2, 0).reshape(B, T, D))
```

```python
import concourse.bass as bass
from concourse import mybir
from contextlib import ExitStack


def gated_recurrence(nc, x, h0, w_state, w_input, bias, out):
    fp32 = mybir.dt.float32
    bf16 = mybir.dt.bfloat16
    ALU = mybir.AluOpType
    ACT = mybir.ActivationFunctionType
    AX = mybir.AxisListType

    P = 128
    B = h0.shape[2]
    KC = h0.shape[1]
    G = KC * B
    T = x.shape[1] // G
    PARTS = 3
    GATES = w_state.shape[2] // (KC * P)
    R, Z, C = range(GATES)
    GROUP = 4
    BLOCK = 2 * GROUP
    NB = T // BLOCK
    HW = 3 * G + 4

    ctx = ExitStack()
    with ctx:
        def sb(name, shape, dt):
            return ctx.enter_context(nc.sbuf_tensor(name, shape, dt))

        def sem(name):
            return ctx.enter_context(nc.semaphore(name))

        X = sb("X", [P, NB + 1, BLOCK * G], fp32)
        xsplit = sb("xsplit", [P, 2, PARTS, GROUP * G], fp32)
        ws32 = sb("ws32", [P, KC, GATES * KC * P], fp32)
        wi32 = sb("wi32", [P, KC, GATES * KC * P], fp32)
        ws = sb("ws", [P, PARTS, KC, GATES * KC * P], bf16)
        wi = sb("wi", [P, PARTS, KC, GATES * KC * P], bf16)
        bias32 = sb("bias32", [P, (GATES + 1) * KC * P], fp32)
        bparts = sb("bparts", [P, PARTS, (GATES + 1) * KC * P], bf16)
        brows = sb("brows", [P, (GATES + 1) * KC * P], bf16)
        ones = sb("ones", [P, GROUP * B], bf16)
        hist = sb("hist", [P, 2, PARTS, HW], fp32)
        h0_sb = sb("h0_sb", [P, G], fp32)
        reset_row = sb("reset_row", [P, 2 * G], fp32)
        memory_row = sb("memory_row", [P, 2, GROUP, 2 * G], fp32)
        warm = sb("warm", [P, 1], fp32)
        update_row = sb("update_row", [P, 3 * G], fp32)

        bank_r = [ctx.enter_context(nc.psum_tensor(f"bank_r{i}", [P, 512], fp32)) for i in range(2)]
        bank_z = [ctx.enter_context(nc.psum_tensor(f"bank_z{i}", [P, 512], fp32)) for i in range(2)]
        bank_c = [ctx.enter_context(nc.psum_tensor(f"bank_c{i}", [P, 512], fp32)) for i in range(2)]
        bank_rm = ctx.enter_context(nc.psum_tensor("bank_rm", [P, 512], fp32))
        reset_sum, memory = bank_rm[:, 0:G], bank_rm[:, 2 * G:4 * G]
        bank_zs = ctx.enter_context(nc.psum_tensor("bank_zs", [P, 512], fp32))
        update_sum = bank_zs[:, 0:G]

        weights_in = [sem(f"weights_in{i}") for i in range(2)]
        small_in = sem("small_in")
        x_in = sem("x_in")
        bias_zeroed = sem("bias_zeroed")
        warm_zeroed = sem("warm_zeroed")
        consts_ready = sem("consts_ready")
        split_act = sem("split_act")
        split_dve = sem("split_dve")
        weights_split = sem("weights_split")
        input_copied = sem("input_copied")
        input_mid = sem("input_mid")
        input_split = sem("input_split")
        candidate_bank_filled = sem("candidate_bank_filled")
        candidate_input_ready = sem("candidate_input_ready")
        state_ready = sem("state_ready")
        mid_ready = sem("mid_ready")
        low_ready = sem("low_ready")
        reset_summed = sem("reset_summed")
        hidden_summed = sem("hidden_summed")
        update_summed = sem("update_summed")
        reset_reduced = sem("reset_reduced")
        memory_operands = sem("memory_operands")
        memory_ready = sem("memory_ready")
        update_reduced = sem("update_reduced")
        candidate_ready = sem("candidate_ready")
        y_ready = sem("y_ready")
        y_out = sem("y_out")

        block = ctx.enter_context(nc.Block())

        def state(q, part=0):
            return hist[:, q, part, 2:2 + 3 * G:3]

        def upper(words):
            return words.bitcast(bf16)[:, 1::2]

        def part_sums(bank, s4):
            return bank[:, s4 * PARTS * G:(s4 + 1) * PARTS * G].rearrange("p (k c) -> p k c", k=PARTS)

        def candidate_input(par):
            return bank_c[par][:, GROUP * PARTS * G:GROUP * (PARTS + 1) * G]

        def state_upper(q, part):
            return hist[:, q, part, :].bitcast(bf16)[:, 5:5 + 6 * G:6]

        @block.sync
        def _(sp):
            sp.dma_start(ws32[:, :, :], w_state).then_inc(weights_in[0], 16)
            sp.dma_start(wi32[:, :, :], w_input).then_inc(weights_in[1], 16)
            for n in range(2):
                sp.dma_start(X[:, n * NB // 2:(n + 1) * NB // 2, :],
                             x[:, n * T * G // 2:(n + 1) * T * G // 2].rearrange("p (n c) -> p n c", c=BLOCK * G)
                             ).then_inc(x_in, 16)
            with sp.Fori(0, NB) as n:
                sp.wait_ge(y_ready, n * BLOCK + BLOCK)
                sp.dma_start(out[:, bass.ds(n * (BLOCK * G), BLOCK * G)],
                             X[:, bass.ds(n, 1), :].rearrange("p a c -> p (a c)")).then_inc(y_out, 16)
            sp.wait_ge(y_out, 16 * NB)

        @block.gpsimd
        def _(pool):
            nc.gpsimd.memset(warm[:, :], 0.0).then_inc(warm_zeroed, 1)
            nc.gpsimd.memset(bias32[:, :], 0.0).then_inc(bias_zeroed, 1)
            nc.gpsimd.memset(brows[:, :], 0.0).then_inc(consts_ready, 1)
            nc.gpsimd.memset(ones[:, :], 1.0).then_inc(consts_ready, 1)
            nc.gpsimd.memset(reset_row[:, :], 0.0).then_inc(consts_ready, 1)
            nc.gpsimd.memset(update_row[:, :], 0.0).then_inc(bias_zeroed, 1)
            pool.wait_ge(bias_zeroed, 2)
            nc.gpsimd.memset(update_row[:, 1::3], -1.0).then_inc(consts_ready, 1)
            nc.gpsimd.memset(X[:, NB, :], 0.0).then_inc(consts_ready, 1)

            with pool.Fori(0, NB) as n:
                for s in range(BLOCK):
                    pool.wait_ge(low_ready, n * BLOCK + (s + 2))
                    y = X[:, bass.ds(n, 1), s * G:(s + 1) * G].rearrange("p a c -> p (a c)")
                    nc.gpsimd.tensor_tensor(y, y, state(1 - s % 2), ALU.add).then_inc(y_ready, 1)
        CONSTS = 5

        @block.scalar
        def _(act):
            act.dma_start(h0_sb[:, :], h0.rearrange("p k b -> p (k b)")).then_inc(small_in, 16)
            act.wait_ge(warm_zeroed, 1)
            nc.scalar.activation(warm[:, :], warm[:, :], ACT.Sigmoid)
            act.wait_ge(bias_zeroed, 1)
            for i in range(PARTS):
                act.dma_start(bias32[32 * i:32 * i + 1, :], bias).then_inc(small_in, 16)

            def first_part(parts, words, done):
                nc.scalar.activation(parts, words, ACT.Copy).then_inc(split_act, 1)

            act.wait_ge(small_in, 16 * (1 + PARTS))
            first_part(bparts[:, 0, :], bias32[:, :], 1)
            act.wait_ge(weights_in[0], 16)
            first_part(ws[:, 0], ws32[:, :, :], 2)
            act.wait_ge(weights_in[1], 16)
            first_part(wi[:, 0], wi32[:, :, :], 3)
            for i, (parts, words) in enumerate([(bparts[:, 1, :], bias32[:, :]), (ws[:, 1], ws32[:, :, :]),
                                                (wi[:, 1], wi32[:, :, :])]):
                act.wait_ge(split_dve, i + 1)
                nc.scalar.activation(parts, words, ACT.Copy).then_inc(split_act, 1)
            act.wait_ge(x_in, 32)
            for g in range(2):
                nc.scalar.activation(xsplit[:, g, 0, :], X[:, 0, g * GROUP * G:(g + 1) * GROUP * G],
                                     ACT.Copy).then_inc(input_copied, 1)
            act.wait_ge(consts_ready, CONSTS)
            act.wait_ge(candidate_bank_filled, 1)
            nc.scalar.activation(memory_row[:, 0, :, 1::2], candidate_input(0), ACT.Copy
                                 ).then_inc(candidate_input_ready, 1)

            with act.Fori(0, NB) as n:
                for s in range(BLOCK):
                    q, par, s4 = s % 2, s // GROUP, s % GROUP
                    if s >= 1:
                        act.wait_ge(y_ready, n * BLOCK + s)
                    if s4 == 1:
                        nc.scalar.activation(
                            xsplit[:, par, 0, :],
                            X[:, bass.ds(n + 1, 1), par * GROUP * G:(par + 1) * GROUP * G].rearrange("p a c -> p (a c)"),
                            ACT.Copy)
                    if s4 == 3:
                        nc.scalar.activation(memory_row[:, 1 - par, :, 1::2], candidate_input(1 - par), ACT.Copy)
                    act.wait_ge(reset_reduced, n * BLOCK + (s + 1))
                    nc.scalar.activation(reset_row[:, 1::2], reset_sum, ACT.Sigmoid).then_inc(memory_operands, 1)
                    act.wait_ge(update_reduced, n * BLOCK + (s + 1))
                    nc.scalar.activation(update_row[:, 2::3], update_sum, ACT.Sigmoid)
                    act.wait_ge(memory_ready, n * BLOCK + (s + 1))
                    nc.scalar.activation(
                        hist[:, q, 0, 1:1 + 3 * G].rearrange("p (g k) -> p g k", k=3)[:, :, 0::2],
                        memory[:, 1::2].unsqueeze(2).to_broadcast([P, G, 2]),
                        ACT.Tanh).then_inc(candidate_ready, 1)

        @block.vector
        def _(dve):
            both = [(bparts[:, 0, :], bparts[:, 1, :], bparts[:, 2, :], bias32[:, :]),
                    (ws[:, 0], ws[:, 1], ws[:, 2], ws32[:, :, :]),
                    (wi[:, 0], wi[:, 1], wi[:, 2], wi32[:, :, :])]
            for i, (hi, mid, lo, words) in enumerate(both):
                dve.wait_ge(split_act, i + 1)
                nc.vector.tensor_tensor(words, words, hi, ALU.subtract).then_inc(split_dve, 1)
            for i, (hi, mid, lo, words) in enumerate(both):
                dve.wait_ge(split_act, len(both) + i + 1)
                nc.vector.tensor_tensor(lo, words, mid, ALU.subtract).then_inc(split_dve, 1)
            dve.wait_ge(split_dve, 2 * len(both))
            dve.wait_ge(consts_ready, CONSTS)
            for i in range(PARTS):
                nc.vector.tensor_copy(brows[32 * i:32 * i + 1, :], bparts[32 * i:32 * i + 1, i, :]
                                      ).then_inc(weights_split, 1)
            for g in range(2):
                dve.wait_ge(input_copied, g + 1)
                nc.vector.tensor_tensor(xsplit[:, g, 1, :], xsplit[:, g, 0, :], upper(xsplit[:, g, 0, :]),
                                        ALU.subtract).then_inc(input_mid, 1)
                dve.wait_ge(input_mid, g + 1)
                nc.vector.tensor_tensor(xsplit[:, g, 2, :], xsplit[:, g, 1, :], upper(xsplit[:, g, 1, :]),
                                        ALU.subtract).then_inc(input_split, 1)
            dve.wait_ge(small_in, 16 * (1 + PARTS))
            nc.vector.tensor_copy(state(0), h0_sb[:, :]).then_inc(state_ready, 1)
            dve.wait_ge(state_ready, 1)
            nc.vector.tensor_tensor(state(0, 1), state(0), state_upper(0, 0), ALU.subtract).then_inc(mid_ready, 1)
            dve.wait_ge(mid_ready, 1)
            nc.vector.tensor_tensor(state(0, 2), state(0, 1), state_upper(0, 1), ALU.subtract).then_inc(low_ready, 1)

            with dve.Fori(0, NB) as n:
                for s in range(BLOCK):
                    q, par, s4, new = s % 2, s // GROUP, s % GROUP, 1 - s % 2
                    both_operands = dve.snap(n * (2 * BLOCK) + 2 * (s + 1))
                    dve.wait_ge(reset_summed, n * BLOCK + (s + 1))
                    nc.vector.tensor_reduce(reset_sum, part_sums(bank_r[par], s4).rearrange("p k c -> p c k"),
                                            AX.X, ALU.add).then_inc(reset_reduced, 1)
                    dve.wait_ge(hidden_summed, n * BLOCK + (s + 1))
                    nc.vector.tensor_reduce(memory_row[:, par, s4, 0::2],
                                            part_sums(bank_c[par], s4).rearrange("p k c -> p c k"),
                                            AX.X, ALU.add).then_inc(memory_operands, 1)
                    dve.wait_ge(update_summed, n * BLOCK + (s + 1))
                    nc.vector.tensor_reduce(update_sum, part_sums(bank_z[par], s4).rearrange("p k c -> p c k"),
                                            AX.X, ALU.add).then_inc(update_reduced, 1)
                    dve.wait_ge(memory_operands, both_operands)
                    nc.vector.tensor_tensor_scan(memory, reset_row[:, :], memory_row[:, par, s4, :], 0.0,
                                                 ALU.mult, ALU.add).then_inc(memory_ready, 1)
                    dve.wait_ge(candidate_ready, n * BLOCK + (s + 1))
                    nc.vector.tensor_tensor_scan(hist[:, new, 0, 0:3 * G], update_row[:, :],
                                                 hist[:, q, 0, 1:1 + 3 * G], 0.0,
                                                 ALU.mult, ALU.add).then_inc(state_ready, 1)
                    dve.wait_ge(state_ready, n * BLOCK + (s + 2))
                    nc.vector.tensor_tensor(state(new, 1), state(new), state_upper(new, 0),
                                            ALU.subtract).then_inc(mid_ready, 1)
                    dve.wait_ge(mid_ready, n * BLOCK + (s + 2))
                    nc.vector.tensor_tensor(state(new, 2), state(new, 1), state_upper(new, 1),
                                            ALU.subtract).then_inc(low_ready, 1)
                    if s4 == 1:
                        nc.vector.tensor_tensor(xsplit[:, par, 1, :], xsplit[:, par, 0, :],
                                                upper(xsplit[:, par, 0, :]), ALU.subtract)
                    if s4 == 2:
                        nc.vector.tensor_tensor(xsplit[:, par, 2, :], xsplit[:, par, 1, :],
                                                upper(xsplit[:, par, 1, :]), ALU.subtract)

        @block.tensor
        def _(pe):
            def weights(w, part, kc, gate, o):
                c = (gate * KC + o) * P
                return w[:, part, kc, c:c + P]

            def state_parts(q, n, kc):
                return hist[:, q, 0:n, :].bitcast(bf16)[:, :, 5 + 6 * B * kc:5 + 6 * B * (kc + 1):6]

            def input_part(g, part, kc):
                return xsplit[:, g, part, :].rearrange("p (t k b) -> p t k b", k=KC, b=B)[:, :, kc, :].bitcast(bf16)[:, :, 1::2]

            def step_sums(bank, s4, n, o):
                return part_sums(bank, s4)[:, 0:n, o * B:(o + 1) * B]

            def group_sums(bank, o):
                return bank[:, 0:GROUP * PARTS * G].rearrange("p (t k c) -> p t k c", k=PARTS, c=G)[:, :, 0, o * B:(o + 1) * B]

            def group_candidates(par, o):
                return candidate_input(par).rearrange("p (t c) -> p t c", c=G)[:, :, o * B:(o + 1) * B]

            PAIRS = [(2, 0), (1, 1), (0, 2), (1, 0), (0, 1), (0, 0)]

            def input_products(g, par):
                HIDDEN, CANDIDATE = 2, 3
                for to, bias_of, gate in ((lambda o: group_sums(bank_c[par], o), HIDDEN, None),
                                          (lambda o: group_candidates(par, o), CANDIDATE, C),
                                          (lambda o: group_sums(bank_r[par], o), R, R),
                                          (lambda o: group_sums(bank_z[par], o), Z, Z)):
                    for o in range(KC):
                        c = (bias_of * KC + o) * P
                        yield to(o), brows[:, c:c + P], ones[:, :], o == 0 and bias_of != CANDIDATE
                    if gate is None:
                        continue
                    for o in range(KC):
                        for kc in range(KC):
                            for i, j in PAIRS:
                                yield to(o), weights(wi, i, kc, gate, o), input_part(g, j, kc), False

            def issue(product):
                to, stationary, moving, first = product
                return nc.tensor.matmul(to, stationary, moving, start=first, stop=True, skip_group_check=True)

            pe.wait_ge(weights_split, PARTS)
            pe.wait_ge(input_split, 2)
            for product in input_products(0, 0):
                last = issue(product)
            last.then_inc(candidate_bank_filled, 1)

            pe.wait_ge(candidate_input_ready, 1)
            with pe.Fori(0, NB) as n:
                for s in range(BLOCK):
                    q, par, s4 = s % 2, s // GROUP, s % GROUP
                    if s4 == 0:
                        ahead = list(input_products(1 - par, 1 - par))
                        each = len(ahead) // GROUP

                    def state_products(bank, gate, i, n):
                        for o in range(KC):
                            for kc in range(KC):
                                last = nc.tensor.matmul(step_sums(bank, s4, n, o), weights(ws, i, kc, gate, o),
                                                        state_parts(q, n, kc), start=False, stop=True,
                                                        skip_group_check=True)
                        return last

                    pe.wait_ge(state_ready, n * BLOCK + (s + 1))
                    state_products(bank_r[par], R, 2, 1)
                    state_products(bank_z[par], Z, 2, 1)
                    pe.wait_ge(mid_ready, n * BLOCK + (s + 1))
                    state_products(bank_r[par], R, 1, 2)
                    state_products(bank_c[par], C, 2, 1)
                    pe.wait_ge(low_ready, n * BLOCK + (s + 1))
                    state_products(bank_r[par], R, 0, 3).then_inc(reset_summed, 1)
                    state_products(bank_c[par], C, 1, 3)
                    state_products(bank_c[par], C, 0, 3).then_inc(hidden_summed, 1)
                    state_products(bank_z[par], Z, 1, 3)
                    state_products(bank_z[par], Z, 0, 3).then_inc(update_summed, 1)
                    for product in ahead[s4 * each:(s4 + 1) * each]:
                        issue(product)


def kernel(x, cond_1024, L0_cond_w_W, L0_cond_w_b, L0_cond_wx_W, L0_cond_wx_b, L0_cond_wh_W, L0_cond_wh_b):
    import numpy as np
    import concourse.bacc as bacc
    from concourse.bass_utils import run_bass_kernel_spmd

    x, h0 = np.asarray(x), np.asarray(cond_1024)
    w_W, w_b = np.asarray(L0_cond_w_W), np.asarray(L0_cond_w_b)
    wx_W, wx_b = np.asarray(L0_cond_wx_W), np.asarray(L0_cond_wx_b)
    wh_W, wh_b = np.asarray(L0_cond_wh_W), np.asarray(L0_cond_wh_b)
    B, T, D = x.shape
    P = 128
    KC = D // P

    def rows(w):
        return np.ascontiguousarray(w.reshape(KC, P, -1).transpose(1, 0, 2))

    arrays = {
        "x": np.ascontiguousarray(x.reshape(B, T, KC, P).transpose(3, 1, 2, 0).reshape(P, T * KC * B)),
        "h0": np.ascontiguousarray(h0.reshape(B, KC, P).transpose(2, 1, 0)),
        "w_state": rows(np.concatenate([w_W[D:], wh_W], axis=1)),
        "w_input": rows(np.concatenate([w_W[:D], wx_W], axis=1)),
        "bias": np.ascontiguousarray(np.concatenate([w_b, wh_b, wx_b])[None, :]),
    }
    nc = bacc.Bacc("TRN2", target_bir_lowering=False, num_devices=1)
    args = [nc.dram_tensor(name, a.shape, mybir.dt.from_np(a.dtype), kind="ExternalInput").ap()
            for name, a in arrays.items()]
    out = nc.dram_tensor("y", arrays["x"].shape, mybir.dt.float32, kind="ExternalOutput").ap()
    gated_recurrence(nc, *args, out)
    r = run_bass_kernel_spmd(nc, [arrays], core_ids=[0])
    y = r.results[0]["y"]
    return np.ascontiguousarray(y.reshape(P, T, KC, B).transpose(3, 1, 2, 0).reshape(B, T, D))
```

```python
import concourse.bass as bass
from concourse import mybir
from contextlib import ExitStack


def gated_recurrence(nc, x, h0, w_state, w_input, bias, out):
    fp32 = mybir.dt.float32
    bf16 = mybir.dt.bfloat16
    ALU = mybir.AluOpType
    ACT = mybir.ActivationFunctionType
    AX = mybir.AxisListType

    P = 128
    B = h0.shape[2]
    KC = h0.shape[1]
    G = KC * B
    T = x.shape[1] // G
    PARTS = 3
    GATES = w_state.shape[2] // (KC * P)
    R, Z, C = range(GATES)
    BIASES = GATES + 1
    HIDDEN, CANDIDATE = 2, 3
    SLOTS = PARTS + 1
    GROUP = 8
    BLOCK = 2 * GROUP
    NB = T // BLOCK

    ctx = ExitStack()
    with ctx:
        def sb(name, shape, dt):
            return ctx.enter_context(nc.sbuf_tensor(name, shape, dt))

        def pb(name):
            return ctx.enter_context(nc.psum_tensor(name, [P, 512], fp32))

        def sem(name):
            return ctx.enter_context(nc.semaphore(name))

        X = sb("X", [P, NB + 1, BLOCK * G], fp32)
        xsplit = sb("xsplit", [P, 2, PARTS, GROUP * G], fp32)
        wi32 = sb("wi32", [P, KC, GATES * KC * P], fp32)
        ws32 = sb("ws32", [P, KC, GATES * KC * P], fp32)
        wi = sb("wi", [P, PARTS, KC, GATES * KC * P], bf16)
        ws = sb("ws", [P, PARTS, KC, GATES * KC * P], bf16)
        bias32 = sb("bias32", [P, P], fp32)
        bparts = sb("bparts", [P, PARTS, P], bf16)
        brows = sb("brows", [P, P], bf16)
        pick = sb("pick", [P, BIASES * KC, GROUP * B], bf16)
        hist = sb("hist", [P, 2, PARTS, 2 * G], fp32)
        h0_sb = sb("h0_sb", [P, G], fp32)
        reset_row = sb("reset_row", [P, SLOTS * G], fp32)
        mix_row = sb("mix_row", [P, 2 * G], fp32)
        update = sb("update", [P, G], fp32)
        warm = sb("warm", [P, 1], fp32)

        bank_r = [pb(f"bank_r{i}") for i in range(2)]
        bank_z = [pb(f"bank_z{i}") for i in range(2)]
        bank_c = [pb(f"bank_c{i}") for i in range(2)]
        chain = pb("bank_chain")[:, 0:(3 + SLOTS) * G]
        reset_sum = chain[:, 0:G]
        candidate_row = chain[:, G:3 * G]
        memory = chain[:, 3 * G:]
        bank_zs = pb("bank_zs")
        update_sum = bank_zs[:, 0:G]

        weights_in = [sem(f"weights_in{k}") for k in range(2 * KC)]
        bias_in, h0_in, x_first_in = sem("bias_in"), sem("h0_in"), sem("x_first_in")
        x_in = sem("x_in")
        warm_zeroed = sem("warm_zeroed")
        zeroed = sem("zeroed")
        rows_filled = sem("rows_filled")
        consts_ready = sem("consts_ready")
        bias_steps = sem("bias_steps")
        first_ready, rest_ready = sem("first_ready"), sem("rest_ready")
        second_ready, third_ready = sem("second_ready"), sem("third_ready")
        input_copied, input_mid, input_split = ([sem(f"input_{step}{g}") for g in range(2)]
                                                for step in ("copied", "mid", "split"))
        state_ready = sem("state_ready")
        mid_ready = sem("mid_ready")
        low_ready = sem("low_ready")
        reset_summed = sem("reset_summed")
        update_summed = sem("update_summed")
        reset_reduced = sem("reset_reduced")
        update_reduced = sem("update_reduced")
        update_ready = sem("update_ready")
        memory_ready = sem("memory_ready")
        y_ready = sem("y_ready")
        memory_operands = sem("memory_operands")
        state_operands = sem("state_operands")
        y_out = sem("y_out")

        CONSTS = 2 * PARTS

        block = ctx.enter_context(nc.Block())

        def state(q, part=0):
            return hist[:, q, part, 1::2]

        def state_upper(q, part):
            return hist[:, q, part, :].bitcast(bf16)[:, 3::4]

        def upper(words):
            return words.bitcast(bf16)[:, 1::2]

        def split_input(engine, nc_engine, g):
            engine.wait_ge(input_copied[g], 1)
            nc_engine.tensor_tensor(xsplit[:, g, 1, :], xsplit[:, g, 0, :], upper(xsplit[:, g, 0, :]),
                                    ALU.subtract).then_inc(input_mid[g], 1)
            engine.wait_ge(input_mid[g], 1)
            nc_engine.tensor_tensor(xsplit[:, g, 2, :], xsplit[:, g, 1, :], upper(xsplit[:, g, 1, :]),
                                    ALU.subtract).then_inc(input_split[g], 1)

        def part_sums(bank, sg):
            return bank[:, sg * PARTS * G:(sg + 1) * PARTS * G].rearrange("p (k c) -> p k c", k=PARTS)

        def memory_sums(par, sg):
            return bank_c[par][:, sg * SLOTS * G:(sg + 1) * SLOTS * G]

        pieces = [(w32[:, kc, :], [w[:, i, kc, :] for i in range(PARTS)], dram[:, kc, :])
                  for w32, w, dram in ((wi32, wi, w_input), (ws32, ws, w_state)) for kc in range(KC)]

        @block.sync
        def _(sp):
            def load(to, n, loaded):
                sp.dma_start(X[:, bass.ds(to, 1), :].rearrange("p a c -> p (a c)"),
                             x[:, bass.ds(n * (BLOCK * G), BLOCK * G)]).then_inc(loaded, 16)

            def store(n):
                sp.wait_ge(y_ready, n * BLOCK + BLOCK)
                sp.dma_start(out[:, bass.ds(n * (BLOCK * G), BLOCK * G)],
                             X[:, bass.ds(n, 1), :].rearrange("p a c -> p (a c)")).then_inc(y_out, 16)

            for k, (words, parts, dram) in enumerate(pieces):
                sp.dma_start(words, dram).then_inc(weights_in[k], 16)
                if k == 0:
                    load(0, 0, x_first_in)
            load(1, 1, x_in)
            with sp.Fori(0, NB - 2) as n:
                sp.wait_ge(x_in, n * 16 + 16)
                load(n + 2, n + 2, x_in)
                store(n)
            sp.wait_ge(x_in, (NB - 1) * 16)
            load(NB, NB - 1, x_in)
            store(NB - 2)
            store(NB - 1)
            sp.wait_ge(y_out, 16 * NB)
            sp.wait_ge(x_in, 16 * NB)

        @block.gpsimd
        def _(pool):
            nc.gpsimd.memset(warm[:, :], 0.0).then_inc(warm_zeroed, 1)
            nc.gpsimd.memset(brows[:, :], 0.0).then_inc(zeroed, 1)
            nc.gpsimd.memset(pick[:, :, :], 0.0).then_inc(zeroed, 1)
            pool.wait_ge(zeroed, 2)
            for i in range(PARTS):
                if i >= 1:
                    pool.wait_ge(consts_ready, i)
                v = pick[32 * i:32 * i + 32, :, :]
                nc.gpsimd.affine_select(out=v, in_=v, compare_op=ALU.not_equal, fill=1.0, base=0,
                                        pattern=[[-1, BIASES * KC], [0, GROUP * B]], channel_multiplier=1
                                        ).then_inc(consts_ready, 1)
            pool.wait_ge(consts_ready, PARTS)
            pool.wait_ge(bias_in, 16)
            nc.gpsimd.tensor_copy(bparts[:, 0, :], bias32[:, :]).then_inc(bias_steps, 1)
            pool.wait_ge(bias_steps, 1)
            nc.gpsimd.tensor_tensor(bias32[:, :], bias32[:, :], bparts[:, 0, :], ALU.subtract).then_inc(bias_steps, 1)
            pool.wait_ge(bias_steps, 2)
            nc.gpsimd.tensor_copy(bparts[:, 1, :], bias32[:, :]).then_inc(bias_steps, 1)
            pool.wait_ge(bias_steps, 3)
            nc.gpsimd.tensor_tensor(bparts[:, 2, :], bias32[:, :], bparts[:, 1, :], ALU.subtract).then_inc(bias_steps, 1)
            pool.wait_ge(bias_steps, 4)
            for i in range(PARTS):
                if i >= 1:
                    pool.wait_ge(consts_ready, PARTS + i)
                rows = slice(32 * i, 32 * i + 32)
                nc.gpsimd.tensor_copy(brows[rows, :], bparts[rows, i, :]).then_inc(consts_ready, 1)

            pool.wait_ge(consts_ready, CONSTS)
            split_input(pool, nc.gpsimd, 1)
            with pool.Fori(0, NB) as n:
                for s in range(BLOCK):
                    pool.wait_ge(low_ready, n * BLOCK + (s + 2))
                    y = X[:, bass.ds(n, 1), s * G:(s + 1) * G].rearrange("p a c -> p (a c)")
                    nc.gpsimd.tensor_tensor(y, y, state(1 - s % 2), ALU.add).then_inc(y_ready, 1)

        @block.scalar
        def _(act):
            act.dma_start(h0_sb[:, :], h0.rearrange("p k b -> p (k b)")).then_inc(h0_in, 16)
            act.dma_start(bias32[:, :], bias).then_inc(bias_in, 16)
            act.wait_ge(warm_zeroed, 1)
            nc.scalar.activation(warm[:, :], warm[:, :], ACT.Sigmoid)
            def copy_input(g):
                nc.scalar.activation(xsplit[:, g, 0, :], X[:, 0, g * GROUP * G:(g + 1) * GROUP * G],
                                     ACT.Copy).then_inc(input_copied[g], 1)

            for first in range(0, len(pieces), KC):
                for k in range(first, first + KC):
                    words, parts, _ = pieces[k]
                    act.wait_ge(weights_in[k], 16)
                    nc.scalar.activation(parts[0], words, ACT.Copy).then_inc(first_ready, 1)
                    if k == 0:
                        act.wait_ge(x_first_in, 16)
                        copy_input(0)
                for k in range(first, first + KC):
                    words, parts, _ = pieces[k]
                    act.wait_ge(rest_ready, k + 1)
                    nc.scalar.activation(parts[1], words, ACT.Copy).then_inc(second_ready, 1)
                    if k == 0:
                        copy_input(1)
            act.wait_ge(rows_filled, 3)

            with act.Fori(0, NB) as n:
                for s in range(BLOCK):
                    q, par, sg = s % 2, s // GROUP, s % GROUP
                    act.wait_ge(reset_reduced, n * BLOCK + (s + 1))
                    nc.scalar.activation(reset_row[:, SLOTS - 1::SLOTS], reset_sum, ACT.Sigmoid
                                         ).then_inc(memory_operands, 1)
                    act.wait_ge(update_reduced, n * BLOCK + (s + 1))
                    nc.scalar.activation(update[:, :], update_sum, ACT.Sigmoid).then_inc(update_ready, 1)
                    if s >= 1:
                        act.wait_ge(y_ready, n * BLOCK + s)
                    nc.scalar.activation(mix_row[:, 0::2], update_sum, ACT.Sigmoid, scale=-1.0)
                    act.wait_ge(memory_ready, n * BLOCK + (s + 1))
                    nc.scalar.activation(candidate_row[:, 1::2], memory[:, SLOTS - 1::SLOTS], ACT.Tanh
                                         ).then_inc(state_operands, 1)
                    if s == 0:
                        act.wait_ge(x_in, n * 16 + 16)
                    if sg == 0:
                        nc.scalar.activation(
                            xsplit[:, par, 0, :],
                            X[:, bass.ds(n + 1, 1), par * GROUP * G:(par + 1) * GROUP * G].rearrange("p a c -> p (a c)"),
                            ACT.Copy)

        @block.vector
        def _(dve):
            nc.vector.memset(candidate_row, 0.0).then_inc(rows_filled, 1)
            nc.vector.memset(reset_row[:, :], 1.0).then_inc(rows_filled, 1)
            dve.wait_ge(rows_filled, 2)
            nc.vector.memset(reset_row[:, 0::SLOTS], 0.0).then_inc(rows_filled, 1)
            dve.wait_ge(h0_in, 16)
            nc.vector.tensor_copy(state(0), h0_sb[:, :]).then_inc(state_ready, 1)
            dve.wait_ge(state_ready, 1)
            nc.vector.tensor_tensor(state(0, 1), state(0), state_upper(0, 0), ALU.subtract).then_inc(mid_ready, 1)
            dve.wait_ge(mid_ready, 1)
            nc.vector.tensor_tensor(state(0, 2), state(0, 1), state_upper(0, 1), ALU.subtract).then_inc(low_ready, 1)
            for first in range(0, len(pieces), KC):
                for k in range(first, first + KC):
                    words, parts, _ = pieces[k]
                    dve.wait_ge(first_ready, k + 1)
                    nc.vector.tensor_tensor(words, words, parts[0], ALU.subtract).then_inc(rest_ready, 1)
                    if k == 0:
                        split_input(dve, nc.vector, 0)
                for k in range(first, first + KC):
                    words, parts, _ = pieces[k]
                    dve.wait_ge(second_ready, k + 1)
                    nc.vector.tensor_tensor(parts[2], words, parts[1], ALU.subtract).then_inc(third_ready, 1)

            with dve.Fori(0, T, BLOCK) as t:
                for s in range(BLOCK):
                    q, par, sg, new = s % 2, s // GROUP, s % GROUP, 1 - s % 2
                    dve.wait_ge(reset_summed, t + (s + 1))
                    nc.vector.tensor_reduce(reset_sum, part_sums(bank_r[par], sg).rearrange("p k c -> p c k"),
                                            AX.X, ALU.add).then_inc(reset_reduced, 1)
                    dve.wait_ge(update_summed, t + (s + 1))
                    nc.vector.tensor_reduce(update_sum, part_sums(bank_z[par], sg).rearrange("p k c -> p c k"),
                                            AX.X, ALU.add).then_inc(update_reduced, 1)
                    two_a_step = dve.snap(t * 2 + 2 * (s + 1))
                    dve.wait_ge(memory_operands, two_a_step)
                    nc.vector.tensor_tensor_scan(memory, reset_row[:, :], memory_sums(par, sg), 0.0,
                                                 ALU.mult, ALU.add).then_inc(memory_ready, 1)
                    dve.wait_ge(update_ready, t + (s + 1))
                    nc.vector.tensor_tensor(mix_row[:, 1::2], update[:, :], state(q), ALU.mult
                                            ).then_inc(state_operands, 1)
                    dve.wait_ge(state_operands, two_a_step)
                    nc.vector.tensor_tensor_scan(hist[:, new, 0, :], candidate_row, mix_row[:, :], 0.0,
                                                 ALU.mult, ALU.add).then_inc(state_ready, 1)
                    dve.wait_ge(state_ready, t + (s + 2))
                    nc.vector.tensor_tensor(state(new, 1), state(new), state_upper(new, 0),
                                            ALU.subtract).then_inc(mid_ready, 1)
                    dve.wait_ge(mid_ready, t + (s + 2))
                    nc.vector.tensor_tensor(state(new, 2), state(new, 1), state_upper(new, 1),
                                            ALU.subtract).then_inc(low_ready, 1)
                    if sg == 1:
                        nc.vector.tensor_tensor(xsplit[:, par, 1, :], xsplit[:, par, 0, :],
                                                upper(xsplit[:, par, 0, :]), ALU.subtract)
                    if sg == 2:
                        nc.vector.tensor_tensor(xsplit[:, par, 2, :], xsplit[:, par, 1, :],
                                                upper(xsplit[:, par, 1, :]), ALU.subtract)

        @block.tensor
        def _(pe):
            def weights(w, part, kc, gate, o):
                c = (gate * KC + o) * P
                return w[:, part, kc, c:c + P]

            def state_parts(q, n, kc):
                return hist[:, q, 0:n, :].bitcast(bf16)[:, :, 3 + 4 * B * kc:4 * B * (kc + 1):4]

            def input_parts(g, first, n, kc):
                words = xsplit[:, g, first:first + n, :].rearrange("p i (t k b) -> p i t k b", k=KC, b=B)[:, :, :, kc, :]
                return words.bitcast(bf16)[:, :, :, 1::2]

            def step_sums(gate, par, sg, n, o):
                if gate == C:
                    return memory_sums(par, sg).rearrange("p (o b k) -> p o k b", o=KC, k=SLOTS)[:, o, 0:n, :]
                return part_sums((bank_r, bank_z)[gate][par], sg)[:, 0:n, o * B:(o + 1) * B]

            def group_sums(bias_of, par, o, n=1):
                if bias_of in (HIDDEN, CANDIDATE):
                    v = bank_c[par][:, 0:GROUP * SLOTS * G].rearrange("p (t o b k) -> p t o b k", o=KC, b=B, k=SLOTS)
                    return v[:, :, o, :, 0 if bias_of == HIDDEN else SLOTS - 1]
                v = (bank_r, bank_z)[bias_of][par][:, 0:GROUP * PARTS * G]
                return v.rearrange("p (t k c) -> p k t c", k=PARTS, c=G)[:, 0:n, :, o * B:(o + 1) * B]

            PAIRS = [(2, 0, 1), (1, 1, 1), (0, 2, 1), (1, 0, 1), (0, 1, 1), (0, 0, 1)]
            SLOT_PAIRS = [(2, 0, 1), (1, 0, 2), (0, 0, 3)]

            def bias_products(par):
                return [(group_sums(bias_of, par, o), brows[:, :], pick[:, bias_of * KC + o, :],
                         o == 0 and bias_of != CANDIDATE)
                        for bias_of in (HIDDEN, CANDIDATE, R, Z) for o in range(KC)]

            def input_products(par, kc):
                return [(group_sums(bias_of, par, o, n), weights(wi, i, kc, gate, o), input_parts(par, j, n, kc), False)
                        for bias_of, gate in ((CANDIDATE, C), (R, R), (Z, Z)) for o in range(KC)
                        for i, j, n in (PAIRS if gate == C else SLOT_PAIRS)]

            def issue(product):
                to, stationary, moving, first = product
                nc.tensor.matmul(to, stationary, moving, start=first, stop=True, skip_group_check=True)

            pe.wait_ge(consts_ready, CONSTS)
            for product in bias_products(0):
                issue(product)
            pe.wait_ge(input_split[0], 1)
            for kc in range(KC):
                pe.wait_ge(third_ready, kc + 1)
                for product in input_products(0, kc):
                    issue(product)
            pe.wait_ge(third_ready, 2 * KC)
            pe.wait_ge(input_split[1], 1)

            with nc.Fori(0, T, BLOCK, engines=[mybir.EngineType.PE], hint_back_edge=True) as t:
                for s in range(BLOCK):
                    q, par, sg = s % 2, s // GROUP, s % GROUP
                    if sg == 0:
                        ahead = bias_products(1 - par)
                        for kc in range(KC):
                            ahead += input_products(1 - par, kc)
                        each = len(ahead) // GROUP

                    def state_products(gate, i, n):
                        for o in range(KC):
                            for kc in range(KC):
                                last = nc.tensor.matmul(step_sums(gate, par, sg, n, o), weights(ws, i, kc, gate, o),
                                                        state_parts(q, n, kc), start=False, stop=True,
                                                        skip_group_check=True)
                        return last

                    pe.wait_ge(state_ready, t + (s + 1))
                    state_products(R, 2, 1)
                    state_products(Z, 2, 1)
                    pe.wait_ge(mid_ready, t + (s + 1))
                    state_products(R, 1, 2)
                    state_products(C, 2, 1)
                    pe.wait_ge(low_ready, t + (s + 1))
                    state_products(R, 0, 3).then_inc(reset_summed, 1)
                    state_products(Z, 1, 3)
                    state_products(Z, 0, 3).then_inc(update_summed, 1)
                    state_products(C, 1, 3)
                    state_products(C, 0, 3).then_inc(memory_operands, 1)
                    for product in ahead[sg * each:(sg + 1) * each]:
                        issue(product)


def kernel(x, cond_1024, L0_cond_w_W, L0_cond_w_b, L0_cond_wx_W, L0_cond_wx_b, L0_cond_wh_W, L0_cond_wh_b):
    import numpy as np
    import concourse.bacc as bacc
    from concourse.bass_utils import run_bass_kernel_spmd

    x, h0 = np.asarray(x), np.asarray(cond_1024)
    w_W, w_b = np.asarray(L0_cond_w_W), np.asarray(L0_cond_w_b)
    wx_W, wx_b = np.asarray(L0_cond_wx_W), np.asarray(L0_cond_wx_b)
    wh_W, wh_b = np.asarray(L0_cond_wh_W), np.asarray(L0_cond_wh_b)
    B, T, D = x.shape
    P = 128
    KC = D // P

    def rows(w):
        return np.ascontiguousarray(w.reshape(KC, P, -1).transpose(1, 0, 2))

    arrays = {
        "x": np.ascontiguousarray(x.reshape(B, T, KC, P).transpose(3, 1, 2, 0).reshape(P, T * KC * B)),
        "h0": np.ascontiguousarray(h0.reshape(B, KC, P).transpose(2, 1, 0)),
        "w_state": rows(np.concatenate([w_W[D:], wh_W], axis=1)),
        "w_input": rows(np.concatenate([w_W[:D], wx_W], axis=1)),
        "bias": np.concatenate([np.pad(b.reshape(-1, P), ((0, 32 - b.size // P), (0, 0)))
                                for b in 3 * [np.concatenate([w_b, wh_b, wx_b])]] + [np.zeros((32, P), w_b.dtype)]),
    }
    nc = bacc.Bacc("TRN2", target_bir_lowering=False, num_devices=1)
    args = [nc.dram_tensor(name, a.shape, mybir.dt.from_np(a.dtype), kind="ExternalInput").ap()
            for name, a in arrays.items()]
    out = nc.dram_tensor("y", arrays["x"].shape, mybir.dt.float32, kind="ExternalOutput").ap()
    gated_recurrence(nc, *args, out)
    r = run_bass_kernel_spmd(nc, [arrays], core_ids=[0])
    y = r.results[0]["y"]
    return np.ascontiguousarray(y.reshape(P, T, KC, B).transpose(3, 1, 2, 0).reshape(B, T, D))
```
